# Optimizing a Trainium2 kernel written in Bass

```python
import numpy as np
import jax
import jax.numpy as jnp

def _softmax(x, axis=-1):
    return jax.nn.softmax(x, axis=axis)

def _gelu(x):
    return jax.nn.gelu(x, approximate=True)

def _silu(x):
    return jax.nn.silu(x)

def _sigmoid(x):
    return jax.nn.sigmoid(x)

def _layernorm(x, axis=-1, eps=1e-05):
    m = jnp.mean(x, axis=axis, keepdims=True)
    v = jnp.var(x, axis=axis, keepdims=True)
    return (x - m) / jnp.sqrt(v + eps)

def _scatter_add(tgt, idx, src, axis=0):
    return tgt.at[idx].add(src)

def _segment_sum(src, seg, n):
    return jax.ops.segment_sum(src, seg, n)
kernel_name = 'mk_xattn_ffn_d1_seqx_r8_4048bf'

def setup_inputs(seed: int=0):
    np.random.seed(seed)
    _w = jnp.asarray

    def _rec_inputs():
        import jax
        import jax.numpy as jnp
        _rk = jax.random.key(seed)
        x = -0.000125 + 0.9999 * jax.random.normal(jax.random.fold_in(_rk, 1), (4, 256, 256), jnp.float32)
        _lenS = 256 - jax.random.randint(jax.random.fold_in(_rk, 7), (4,), 0, max(1, 256 // 4) + 1, jnp.int32)
        _lenS2 = 256 - jax.random.randint(jax.random.fold_in(_rk, 8), (4,), 0, max(1, 256 // 4) + 1, jnp.int32)
        itok_BxS_13_99985 = jax.random.randint(jax.random.fold_in(_rk, 11), (4, 256), 13, 99986, jnp.int32)
        _ctx_2048P = jax.random.normal(jax.random.fold_in(_rk, 12), (4, 16, 256), jnp.float32)
        _ctx_2048c = jax.random.dirichlet(jax.random.fold_in(_rk, 512), 0.3 * jnp.ones((16,), jnp.float32), (4, 256))
        _ctx_2048t = jnp.einsum('bsk,bkd->bsd', _ctx_2048c, _ctx_2048P)
        _ctx_2048t = _ctx_2048t * jax.lax.rsqrt(jnp.mean(jnp.square(_ctx_2048t)) + 1e-12) * 0.953939
        ctx_2048 = 6.82029e-06 + 0.0200006 * (_ctx_2048t + 0.3 * jax.random.normal(jax.random.fold_in(_rk, 612), (4, 256, 256), jnp.float32))
        return (x, itok_BxS_13_99985, ctx_2048)
    x, itok_BxS_13_99985, ctx_2048 = _rec_inputs()

    def _L0_xattn_setup():
        import jax, jax.numpy as jnp
        import numpy as np
        B, S, D = (4, 512, 256)
        E = 4
        F = 1024 // E
        VOCAB = 12500
        key = jax.random.key(seed)
        k1, k2, k3, k4, k5 = jax.random.split(key, 5)
        hidden_states = jax.random.normal(k1, (B, S, D), dtype=jnp.float32)
        token_ids = jax.random.randint(k2, (B, S), 0, VOCAB, dtype=jnp.int64)
        Wg = jax.random.normal(k3, (E, F, D), dtype=jnp.float32) * 0.02
        Wu = jax.random.normal(k4, (E, F, D), dtype=jnp.float32) * 0.02
        Wd = jax.random.normal(k5, (E, D, F), dtype=jnp.float32) * 0.02
        return {'hidden_states': hidden_states, 'token_ids': token_ids, 'Wg': Wg, 'Wu': Wu, 'Wd': Wd}
    _L0_xattn_all = _L0_xattn_setup()
    _L0_xattn_in = {k: v for k, v in _L0_xattn_all.items() if k in ()}
    del _L0_xattn_all

    def _L0_ffn_setup():
        import jax, jax.numpy as jnp
        import numpy as np
        TOP_K = 2
        key = jax.random.key(seed)
        ks = jax.random.split(key, 5)
        B, T, D, E, H = (4, 256, 256, 8, 176)
        s = 1.0 / np.sqrt(D)
        sh = 1.0 / np.sqrt(H)
        return {'x': jax.random.normal(ks[0], (B, T, D), dtype=jnp.float32), 'Wg': jax.random.normal(ks[1], (E, D), dtype=jnp.float32) * s, 'W1': jax.random.normal(ks[2], (E, H, D), dtype=jnp.float32) * s, 'W2': jax.random.normal(ks[3], (E, H, D), dtype=jnp.float32) * s, 'W3': jax.random.normal(ks[4], (E, D, H), dtype=jnp.float32) * sh}
    _L0_ffn_all = _L0_ffn_setup()
    _L0_ffn_in = {k: v for k, v in _L0_ffn_all.items() if k in ('Wg', 'W1', 'W2', 'W3')}
    del _L0_ffn_all
    return {'x': x, 'itok_BxS_13_99985': itok_BxS_13_99985, 'ctx_2048': ctx_2048, 'L0_ffn_Wg': _L0_ffn_in['Wg'], 'L0_ffn_W1': _L0_ffn_in['W1'], 'L0_ffn_W2': _L0_ffn_in['W2'], 'L0_ffn_W3': _L0_ffn_in['W3']}

def reference(x, itok_BxS_13_99985, ctx_2048, L0_ffn_Wg, L0_ffn_W1, L0_ffn_W2, L0_ffn_W3):
    import jax
    import jax.numpy as jnp

    def _L0_xattn_ref(hidden_states, token_ids, Wg, Wu, Wd):
        import jax, jax.numpy as jnp
        import numpy as np
        B, S, D = (4, 512, 256)
        E = 4
        F = 1024 // E
        VOCAB = 12500
        tokens_per_expert = VOCAB // E
        tid = jnp.clip(token_ids, 0, VOCAB - 1)
        expert_ids = jnp.minimum(tid // tokens_per_expert, E - 1)
        out = jnp.zeros_like(hidden_states)
        for e in range(E):
            g = jax.nn.silu(jnp.einsum('bsd,fd->bsf', hidden_states, Wg[e]))
            u = jnp.einsum('bsd,fd->bsf', hidden_states, Wu[e])
            y = jnp.einsum('bsf,df->bsd', g * u, Wd[e])
            out = jnp.where((expert_ids == e)[..., None], y, out)
        return out

    def _L0_ffn_ref(x, Wg, W1, W2, W3):
        import jax, jax.numpy as jnp
        import numpy as np
        TOP_K = 2
        E = Wg.shape[0]
        scores = jnp.einsum('btd,ed->bte', x, Wg)
        topk_s, topk_i = jax.lax.top_k(scores, TOP_K)
        probs = jax.nn.softmax(topk_s, axis=-1)
        onehot = (topk_i[..., None] == jnp.arange(E)).astype(x.dtype)
        w = jnp.einsum('btk,btke->bte', probs, onehot)
        y = jnp.zeros_like(x)
        for e in range(E):
            h = jax.nn.silu(jnp.einsum('btd,hd->bth', x, W1[e])) * jnp.einsum('btd,hd->bth', x, W2[e])
            y = y + w[..., e:e + 1] * jnp.einsum('bth,dh->btd', h, W3[e])
        return y
    x = x + _L0_xattn_ref(_layernorm(x, axis=-1), itok_BxS_13_99985, ctx_2048, ctx_2048, ctx_2048)
    x = x + _L0_ffn_ref(_layernorm(x, axis=-1), L0_ffn_Wg, L0_ffn_W1, L0_ffn_W2, L0_ffn_W3)
    return x

_drawn_inputs = setup_inputs


def setup_inputs(seed=0):
    import zlib

    import numpy as np

    out = dict(_drawn_inputs(seed))
    spreads = {}
    factors = {}
    for name, (base, spread) in spreads.items():
        noise = np.random.default_rng([zlib.crc32(name.encode()), seed]).standard_normal(out[name].shape)
        drawn = base * np.exp(spread * noise) if base else spread * noise
        out[name] = jnp.asarray(drawn.astype(out[name].dtype))
    for name, factor in factors.items():
        out[name] = (out[name] * factor).astype(out[name].dtype)
    return out
```

```python
from contextlib import ExitStack

import concourse.bass as bass
from concourse import mybir
from concourse.alu_op_type import AluOpType as ALU

F32 = mybir.dt.float32
F32R = mybir.dt.float32r
I32 = mybir.dt.int32
U32 = mybir.dt.uint32
ACT = mybir.ActivationFunctionType

P = 128
TOKENS, D = 1024, 256
TILES = TOKENS // P
HALF_TILES = TILES // 2
HALF = HALF_TILES * P
KD = D // P
VOCAB, EXPERTS1, FF1 = 12500, 4, 256
EXPERTS2, FF2 = 8, 176
CHUNKS = (EXPERTS1 * FF1 // P, EXPERTS2 * FF2 // P)
ROWS = (P // EXPERTS1, P // EXPERTS2)
UPS = (1, 2)
UP_COLS = tuple(n * KD * P for n in UPS)
PIECE = tuple(n + D for n in UP_COLS)
LAG = 2
EPS = 1e-5
RING = 8
RSQRT_SEED = 0x5F3759DF
NEWTON_STEPS = 3
PER_EXPERT = VOCAB // EXPERTS1

STEPS = [(b, h, c) for b in range(2) for h in range(2) for c in range(CHUNKS[b])]
FIRST = {(b, h): STEPS.index((b, h, 0)) for b in range(2) for h in range(2)}
LAST = {(b, h): FIRST[b, h] + CHUNKS[b] - 1 for b in range(2) for h in range(2)}
NSTEPS = len(STEPS)

C_IDENT, C_EXPERT, C_IOTA = 0, P, 2 * P
CONSTS = 2 * P + EXPERTS2


def ffn_moe(nc, x, token_ids, weights1, weights2, router, consts, out):
    x_v = x.rearrange("(p t) d -> p t d", t=TILES)
    out_v = out.rearrange("(p t) d -> p t d", t=TILES)

    ctx = ExitStack()
    with ctx:
        def sb(name, shape, dt=F32):
            return ctx.enter_context(nc.sbuf_tensor(name, shape, dt))

        def sem(name):
            return ctx.enter_context(nc.semaphore(name))

        x_sb = sb("x_sb", [P, TILES, D])
        x2_sb = sb("x2_sb", [P, TILES, D])
        norm = sb("norm", [P, HALF_TILES, D])
        out_sb = x_sb
        ids_sb = sb("ids_sb", [P, TILES], I32)
        consts_sb = sb("consts_sb", [P, CONSTS])
        router_raw = sb("router_raw", [P, KD, EXPERTS2])
        router_hl = sb("router_hl", [P, KD, 2, EXPERTS2], F32R)
        raw = sb("raw", [P, RING, PIECE[1]])
        w_hi = (sb("w_hi1", [P, CHUNKS[0], PIECE[0]], F32R), sb("w_hi2", [P, CHUNKS[1], PIECE[1]], F32R))
        w_lo = (sb("w_lo1", [P, CHUNKS[0], PIECE[0]], F32R), sb("w_lo2", [P, CHUNKS[1], PIECE[1]], F32R))
        hT_hi = sb("hT_hi", [P, 2, KD, HALF], F32R)
        hT_lo = sb("hT_lo", [P, 2, KD, HALF], F32R)
        gate = sb("gate", [P, 2, HALF])
        gate_rows = sb("gate_rows", [P, TILES, P])
        silu = sb("silu", [P, 2, HALF])
        gated = sb("gated", [P, 2, HALF])
        act = sb("act", [P, 2, HALF])
        act_hi = sb("act_hi", [P, 2, HALF], F32R)
        act_lo = sb("act_lo", [P, 2, HALF], F32R)
        over = sb("over", [P, 3, TILES])
        expert = sb("expert", [P, TILES])
        stats = sb("stats", [P, TILES, 6])
        mv = sb("mv", [P, HALF_TILES, 2])
        var = sb("var", [P, HALF_TILES])
        seed = sb("seed", [P, HALF_TILES], I32)
        rstd = sb("rstd", [P, HALF_TILES])
        newton = sb("newton", [P, HALF_TILES])
        score_part = sb("score_part", [P, HALF_TILES, EXPERTS2])
        score = sb("score", [P, HALF_TILES, EXPERTS2])
        top = sb("top", [P, HALF_TILES, 8])
        top_i = sb("top_i", [P, HALF_TILES, 8], U32)
        gap = sb("gap", [P, HALF_TILES])
        th = sb("th", [P, HALF_TILES])
        prob = sb("prob", [P, 2, HALF_TILES])
        pick = sb("pick", [P, 2, HALF_TILES, EXPERTS2])
        w_tok = sb("w_tok", [P, HALF_TILES, EXPERTS2])

        z = [ctx.enter_context(nc.psum_tensor(f"z{i}", [P, HALF], F32)) for i in range(4)]
        y = [[ctx.enter_context(nc.psum_tensor(f"y{h}{i}", [P, 2 * D], F32)) for i in range(2)] for h in range(2)]

        x_in = [sem(f"x_in{h}") for h in range(2)]
        ids_in, consts_in, router_in = sem("ids_in"), sem("consts_in"), sem("router_in")
        w_in = [[sem(f"w_in{b}_{c}") for c in range(CHUNKS[b])] for b in range(2)]
        w_hi_done, w_lo_done, router_split = sem("w_hi_done"), sem("w_lo_done"), sem("router_split")
        pool_chain, dve_chain = sem("pool_chain"), sem("dve_chain")
        gate_rows_done = sem("gate_rows_done")
        gate_T, gate_done = sem("gate_T"), sem("gate_done")
        norm_done, norm_T, hT_hi_done, hT_lo_done = sem("norm_done"), sem("norm_T"), sem("hT_hi_done"), sem("hT_lo_done")
        scored, gap_done, th_done = sem("scored"), sem("gap_done"), sem("th_done")
        up_done, silu_done, gated_done, act_done = sem("up_done"), sem("silu_done"), sem("gated_done"), sem("act_done")
        act_hi_done, act_lo_done, down_done = sem("act_hi_done"), sem("act_lo_done"), sem("down_done")
        y_read, out_ready, stored = sem("y_read"), sem("out_ready"), sem("stored")

        block = ctx.enter_context(nc.Block())

        ident = consts_sb[:, C_IDENT:C_IDENT + P]
        expert_row = consts_sb[:, C_EXPERT:C_EXPERT + P]
        iota = consts_sb[:, C_IOTA:C_IOTA + EXPERTS2]

        def piece_no(b, c):
            return b * CHUNKS[0] + c + 1

        def raw_piece(b, c):
            return raw[:, (piece_no(b, c) - 1) % RING, 0:PIECE[b]]

        def ln_no(b, h):
            return 2 * b + h

        def tiles_of(h):
            return range(h * HALF_TILES, (h + 1) * HALF_TILES)

        @block.sync
        def _(sp):
            def load_piece(b, c):
                if piece_no(b, c) > RING:
                    sp.wait_ge(w_lo_done, piece_no(b, c) - RING)
                sp.dma_start(raw_piece(b, c), (weights1, weights2)[b][:, c, :]).then_inc(w_in[b][c], 16)

            sp.dma_start(x_sb[:, 0:HALF_TILES, :], x_v[:, 0:HALF_TILES, :]).then_inc(x_in[0], 16)
            sp.dma_start(consts_sb[:], consts).then_inc(consts_in, 16)
            sp.dma_start(ids_sb[:], token_ids).then_inc(ids_in, 16)
            for c in range(3):
                load_piece(0, c)
            sp.dma_start(x_sb[:, HALF_TILES:, :], x_v[:, HALF_TILES:, :]).then_inc(x_in[1], 16)
            for c in range(3, CHUNKS[0]):
                load_piece(0, c)
            sp.dma_start(router_raw[:], router).then_inc(router_in, 16)
            for c in range(CHUNKS[1]):
                load_piece(1, c)
            for n in range(4):
                sp.wait_ge(out_ready, n + 1)
                sp.dma_start(out_v[:, 2 * n:2 * n + 2, :], out_sb[:, 2 * n:2 * n + 2, :]).then_inc(stored, 16)
            sp.wait_ge(stored, 64)

        @block.gpsimd
        def _(pool):
            def weight_lo(b, c):
                pool.wait_ge(w_hi_done, piece_no(b, c))
                nc.gpsimd.tensor_tensor(w_lo[b][:, c, :], raw_piece(b, c), w_hi[b][:, c, :].bitcast(F32),
                                        ALU.subtract).then_inc(w_lo_done, 1)

            pool.wait_ge(ids_in, 16)
            for e in range(1, EXPERTS1):
                nc.gpsimd.tensor_scalar(over[:, e - 1, :], ids_sb[:], float(e * PER_EXPERT), None, ALU.is_ge)\
                    .then_inc(pool_chain, 1)
            pool.wait_ge(pool_chain, 3)
            nc.gpsimd.tensor_tensor(expert[:], over[:, 0, :], over[:, 1, :], ALU.add).then_inc(pool_chain, 1)
            pool.wait_ge(pool_chain, 4)
            nc.gpsimd.tensor_tensor(expert[:], expert[:], over[:, 2, :], ALU.add).then_inc(pool_chain, 1)
            pool.wait_ge(pool_chain, 5)
            pool.wait_ge(consts_in, 16)
            for t in range(TILES):
                nc.gpsimd.tensor_scalar(gate_rows[:, t, :], expert_row, expert[:, t:t + 1], None, ALU.is_equal)\
                    .then_inc(gate_rows_done, 1)
            weight_lo(0, 0)
            weight_lo(0, 1)
            for q, (b, h, c) in enumerate(STEPS):
                pool.wait_ge(silu_done, q + 1)
                if q >= 2:
                    pool.wait_ge(act_done, q - 1)
                if c == 0:
                    pool.wait_ge(gate_done, ln_no(b, h) + 1)
                nc.gpsimd.tensor_tensor(gated[:, q % 2, :], silu[:, q % 2, :], gate[:, h, :], ALU.mult)\
                    .then_inc(gated_done, 1)
                n = q + 2
                if n < CHUNKS[0]:
                    weight_lo(0, n)
                elif n < CHUNKS[0] + CHUNKS[1]:
                    weight_lo(1, n - CHUNKS[0])

        @block.scalar
        def _(act_e):
            def weight_hi(b, c):
                act_e.wait_ge(w_in[b][c], 16)
                nc.scalar.copy(w_hi[b][:, c, :], raw_piece(b, c)).then_inc(w_hi_done, 1)

            def tokens_hi(b, h):
                for k in range(KD):
                    act_e.wait_ge(norm_T, KD * ln_no(b, h) + k + 1)
                    if b == 1 and k == 0:
                        act_e.wait_ge(up_done, LAST[0, h] + 1)
                    nc.scalar.copy(hT_hi[:, h, k, :], y[h][k][:]).then_inc(hT_hi_done, 1)

            def gates_out(b, h):
                act_e.wait_ge(gate_T, ln_no(b, h) + 1)
                if b == 1:
                    act_e.wait_ge(gated_done, LAST[0, h] + 1)
                nc.scalar.copy(gate[:, h, :], y[h][0][:]).then_inc(gate_done, 1)

            def round_act(q):
                act_e.wait_ge(act_done, q + 1)
                if q >= 2:
                    act_e.wait_ge(down_done, q - 1)
                nc.scalar.copy(act_hi[:, q % 2, :], act[:, q % 2, :]).then_inc(act_hi_done, 1)

            weight_hi(0, 0)
            weight_hi(0, 1)
            gates_out(0, 0)
            gates_out(0, 1)
            tokens_hi(0, 0)
            for q, (b, h, c) in enumerate(STEPS):
                act_e.wait_ge(up_done, q + 1)
                if q >= 2:
                    act_e.wait_ge(gated_done, q - 1)
                nc.scalar.activation(silu[:, q % 2, :], z[2 * (q % 2)][:], ACT.Silu).then_inc(silu_done, 1)
                if q >= 1:
                    round_act(q - 1)
                if (b, h, c) == (0, 0, 1):
                    act_e.wait_ge(router_in, 16)
                    nc.scalar.copy(router_hl[:, :, 0, :], router_raw[:]).then_inc(router_split, 1)
                if (b, h, c) == (0, 0, 3):
                    tokens_hi(0, 1)
                for hh, q0 in ((0, FIRST[0, 1]), (1, FIRST[1, 0])):
                    if q == q0 + 5:
                        tokens_hi(1, hh)
                    if q == q0 + 6:
                        act_e.wait_ge(gap_done, hh + 1)
                        nc.scalar.activation(th[:], gap[:], ACT.Tanh, scale=0.5).then_inc(th_done, 1)
                    if q == q0 + 7:
                        gates_out(1, hh)
                n = q + 2
                if n < CHUNKS[0]:
                    weight_hi(0, n)
                elif n < CHUNKS[0] + CHUNKS[1]:
                    weight_hi(1, n - CHUNKS[0])
            round_act(NSTEPS - 1)

        @block.vector
        def _(dve):
            chain = [0]

            def link(ins):
                chain[0] += 1
                ins.then_inc(dve_chain, 1)
                dve.wait_ge(dve_chain, chain[0])

            def normalise(b, h, src):
                tiles = tiles_of(h)
                for t in tiles:
                    last = nc.vector.bn_stats(stats[:, t, :], src[:, t, :])
                link(last)
                for i, t in enumerate(tiles):
                    last = nc.vector.bn_aggr(mv[:, i, :], stats[:, t, :])
                link(last)
                link(nc.vector.tensor_scalar(var[:], mv[:, :, 1], EPS, None, ALU.add))
                link(nc.vector.tensor_scalar(seed[:], var[:].bitcast(I32), 1, None, ALU.logical_shift_right))
                link(nc.vector.tensor_scalar(rstd[:].bitcast(I32), seed[:], -1.0, float(RSQRT_SEED), ALU.mult, ALU.add))
                for _ in range(NEWTON_STEPS):
                    link(nc.vector.tensor_tensor(newton[:], rstd[:], rstd[:], ALU.mult))
                    link(nc.vector.tensor_tensor(newton[:], newton[:], var[:], ALU.mult))
                    link(nc.vector.tensor_scalar(newton[:], newton[:], -0.5, 1.5, ALU.mult, ALU.add))
                    link(nc.vector.tensor_tensor(rstd[:], rstd[:], newton[:], ALU.mult))
                if ln_no(b, h):
                    dve.wait_ge(norm_T, KD * ln_no(b, h))
                for i, t in enumerate(tiles):
                    nc.vector.tensor_scalar(norm[:, i, :], src[:, t, :], mv[:, i, 0:1], rstd[:, i:i + 1],
                                            ALU.subtract, ALU.mult).then_inc(norm_done, 1)

            def tokens_lo(b, h):
                for k in range(KD):
                    dve.wait_ge(hT_hi_done, KD * ln_no(b, h) + k + 1)
                    nc.vector.tensor_tensor(hT_lo[:, h, k, :], y[h][k][:], hT_hi[:, h, k, :].bitcast(F32),
                                            ALU.subtract).then_inc(hT_lo_done, 1)

            def add_block(b, h, src, dst, done):
                dve.wait_ge(down_done, LAST[b, h] + 1)
                for i in range(2):
                    t = h * HALF_TILES + 2 * i
                    ins = nc.vector.tensor_tensor(dst[:, t:t + 2, :].rearrange("p t d -> p (t d)"), y[h][i][:],
                                                  src[:, t:t + 2, :].rearrange("p t d -> p (t d)"), ALU.add)
                    ins.then_inc(done, 1)

            def route(h):
                dve.wait_ge(scored, h + 1)
                sc = y[h][0][:, 0:HALF_TILES * 2 * EXPERTS2].rearrange("p (t a e) -> p t a e", a=2, e=EXPERTS2)
                link(nc.vector.tensor_copy(score_part[:], sc[:, :, 1, :]))
                link(nc.vector.tensor_tensor(score[:], sc[:, :, 0, :], score_part[:], ALU.add))
                for i in range(HALF_TILES):
                    last = nc.vector.max(top[:, i, :], score[:, i, :])
                link(last)
                for i in range(HALF_TILES):
                    last = nc.vector.max_index(top_i[:, i, :], top[:, i, :], score[:, i, :])
                link(last)
                nc.vector.tensor_tensor(gap[:], top[:, :, 1], top[:, :, 0], ALU.subtract).then_inc(gap_done, 1)
                for j in range(2):
                    last = nc.vector.tensor_tensor(
                        pick[:, j, :, :], iota.unsqueeze(1).to_broadcast([P, HALF_TILES, EXPERTS2]),
                        top_i[:, :, j:j + 1].to_broadcast([P, HALF_TILES, EXPERTS2]), ALU.is_equal)
                link(last)
                dve.wait_ge(th_done, h + 1)
                for j, s in enumerate((-0.5, 0.5)):
                    last = nc.vector.tensor_scalar(prob[:, j, :], th[:], s, 0.5, ALU.mult, ALU.add)
                link(last)
                for j in range(2):
                    last = nc.vector.tensor_tensor(
                        pick[:, j, :, :], pick[:, j, :, :],
                        prob[:, j, :].unsqueeze(2).to_broadcast([P, HALF_TILES, EXPERTS2]), ALU.mult)
                link(last)
                link(nc.vector.tensor_tensor(w_tok[:], pick[:, 0, :, :], pick[:, 1, :, :], ALU.add))
                for i, t in enumerate(tiles_of(h)):
                    nc.vector.tensor_copy(gate_rows[:, t, :].rearrange("p (e r) -> p e r", r=ROWS[1]),
                                          w_tok[:, i, :].unsqueeze(2).to_broadcast([P, EXPERTS2, ROWS[1]]))\
                        .then_inc(gate_rows_done, 1)

            def act_low(q):
                dve.wait_ge(act_hi_done, q + 1)
                if q >= 2:
                    dve.wait_ge(down_done, q - 1)
                nc.vector.tensor_tensor(act_lo[:, q % 2, :], act[:, q % 2, :], act_hi[:, q % 2, :].bitcast(F32),
                                        ALU.subtract).then_inc(act_lo_done, 1)

            dve.wait_ge(x_in[0], 16)
            normalise(0, 0, x_sb)
            tokens_lo(0, 0)
            dve.wait_ge(x_in[1], 16)
            for q, (b, h, c) in enumerate(STEPS):
                if q >= 1:
                    act_low(q - 1)
                dve.wait_ge(gated_done, q + 1)
                nc.vector.tensor_tensor(act[:, q % 2, :], gated[:, q % 2, :], z[2 * (q % 2) + b][:], ALU.mult)\
                    .then_inc(act_done, 1)
                if q == 1:
                    normalise(0, 1, x_sb)
                if q == 2:
                    dve.wait_ge(router_split, 1)
                    nc.vector.tensor_tensor(router_hl[:, :, 1, :], router_raw[:], router_hl[:, :, 0, :].bitcast(F32),
                                            ALU.subtract).then_inc(router_split, 1)
                if q == 3:
                    tokens_lo(0, 1)
                for hh, q0 in ((0, FIRST[0, 1]), (1, FIRST[1, 0])):
                    if q == q0 + 2:
                        add_block(0, hh, x_sb, x2_sb, y_read)
                        dve.wait_ge(y_read, 2 * hh + 2)
                        normalise(1, hh, x2_sb)
                    if q == q0 + 5:
                        tokens_lo(1, hh)
                        route(hh)
                if q == LAST[1, 0] + 3:
                    add_block(1, 0, x2_sb, out_sb, out_ready)
            act_low(NSTEPS - 1)
            add_block(1, 1, x2_sb, out_sb, out_ready)

        @block.tensor
        def _(pe):
            def transpose_gates(b, h, bank):
                for i, t in enumerate(tiles_of(h)):
                    pe.wait_ge(gate_rows_done, b * TILES + t + 1)
                    last = nc.tensor.transpose(bank[:, i * P:(i + 1) * P], gate_rows[:, t, :], ident)
                last.then_inc(gate_T, 1)

            def transpose_tokens(b, h):
                for k in range(KD):
                    for i in range(HALF_TILES):
                        pe.wait_ge(norm_done, HALF_TILES * ln_no(b, h) + i + 1)
                        last = nc.tensor.transpose(y[h][k][:, i * P:(i + 1) * P], norm[:, i, k * P:(k + 1) * P], ident)
                    last.then_inc(norm_T, 1)

            def route_scores(h):
                pe.wait_ge(hT_lo_done, KD * ln_no(1, h) + KD)
                pe.wait_ge(router_split, 2)
                for i in range(HALF_TILES):
                    cols = slice(i * P, (i + 1) * P)
                    o = y[h][0][:, i * 2 * EXPERTS2:(i + 1) * 2 * EXPERTS2]
                    for j, k in enumerate((0, 1)):
                        if k == KD - 1:
                            for kk in range(KD):
                                nc.tensor.matmul(o[:, 0:EXPERTS2], hT_lo[:, h, kk, cols], router_hl[:, kk, 0, :],
                                                 start=False, stop=False)
                        last = nc.tensor.matmul(o, hT_hi[:, h, k, cols],
                                                router_hl[:, k, :, :].rearrange("p a e -> p (a e)"),
                                                start=(k == 0), stop=(k == KD - 1))
                last.then_inc(scored, 1)

            def up(q):
                b, h, c = STEPS[q]
                pe.wait_ge(w_lo_done, piece_no(b, c))
                if c == 0:
                    pe.wait_ge(hT_lo_done, KD * ln_no(b, h) + KD)
                if q >= 2:
                    pe.wait_ge(act_done, q - 1)
                for m in range(UPS[b]):
                    bank = z[2 * (q % 2) + m]
                    for k in range(KD):
                        cols = slice((m * KD + k) * P, (m * KD + k + 1) * P)
                        nc.tensor.matmul(bank[:], w_lo[b][:, c, cols], hT_hi[:, h, k, :], start=(k == 0), stop=False)
                        nc.tensor.matmul(bank[:], w_hi[b][:, c, cols], hT_lo[:, h, k, :], start=False, stop=False)
                        last = nc.tensor.matmul(bank[:], w_hi[b][:, c, cols], hT_hi[:, h, k, :], start=False,
                                                stop=(k == KD - 1))
                last.then_inc(up_done, 1)

            def down(q):
                b, h, c = STEPS[q]
                pe.wait_ge(act_lo_done, q + 1)
                wd = slice(UP_COLS[b], PIECE[b])
                for i in range(HALF_TILES):
                    rows = slice(i * P, (i + 1) * P)
                    o = y[h][i // 2][:, (i % 2) * D:(i % 2 + 1) * D]
                    first = c == 0 and i % 2 == 0
                    for j, (a, w) in enumerate(((act_lo, w_hi), (act_hi, w_lo), (act_hi, w_hi))):
                        last = nc.tensor.matmul(o, a[:, q % 2, rows], w[b][:, c, wd], start=(first and j == 0),
                                                stop=(c == CHUNKS[b] - 1 and j == 2), skip_group_check=True)
                last.then_inc(down_done, 1)

            pe.wait_ge(consts_in, 16)
            transpose_gates(0, 0, y[0][0])
            transpose_gates(0, 1, y[1][0])
            pe.wait_ge(gate_done, 1)
            transpose_tokens(0, 0)
            for q in range(NSTEPS + LAG):
                if q == 3:
                    pe.wait_ge(gate_done, 2)
                    transpose_tokens(0, 1)
                for hh, q0 in ((0, FIRST[0, 1]), (1, FIRST[1, 0])):
                    if q == q0 + 5:
                        pe.wait_ge(y_read, 2 * hh + 2)
                        transpose_tokens(1, hh)
                    if q == q0 + 6:
                        route_scores(hh)
                    if q == q0 + 7:
                        transpose_gates(1, hh, y[hh][0])
                if q < NSTEPS:
                    up(q)
                if q >= LAG:
                    b, h, c = STEPS[q - LAG]
                    if c == 0:
                        if b == 0:
                            pe.wait_ge(hT_lo_done, KD * ln_no(0, h) + KD)
                        else:
                            pe.wait_ge(gate_done, ln_no(1, h) + 1)
                    down(q - LAG)


def kernel(x, itok_BxS_13_99985, ctx_2048, L0_ffn_Wg, L0_ffn_W1, L0_ffn_W2, L0_ffn_W3):
    import numpy as np
    import concourse.bacc as bacc
    from concourse.bass_utils import run_bass_kernel_spmd

    c1, c2 = CHUNKS
    ctx = np.asarray(ctx_2048)
    up1 = ctx.reshape(EXPERTS1, c1, ROWS[0], KD, P).transpose(4, 1, 3, 0, 2).reshape(P, c1, KD * P)
    down1 = ctx.reshape(EXPERTS1, D, c1, ROWS[0]).transpose(0, 3, 2, 1).reshape(P, c1, D)
    ups2 = [np.asarray(w).reshape(EXPERTS2, c2, ROWS[1], KD, P).transpose(4, 1, 3, 0, 2).reshape(P, c2, KD * P)
            for w in (L0_ffn_W1, L0_ffn_W2)]
    down2 = np.asarray(L0_ffn_W3).reshape(EXPERTS2, D, c2, ROWS[1]).transpose(0, 3, 2, 1).reshape(P, c2, D)
    consts = np.zeros((P, CONSTS), np.float32)
    consts[:, C_IDENT:C_IDENT + P] = np.eye(P)
    consts[:, C_EXPERT:C_EXPERT + P] = np.arange(P) // ROWS[0]
    consts[:, C_IOTA:] = np.arange(EXPERTS2)
    arrays = {
        "x_dram": np.ascontiguousarray(np.asarray(x).reshape(TOKENS, D)),
        "token_ids_dram": np.ascontiguousarray(np.asarray(itok_BxS_13_99985).reshape(P, TILES)),
        "weights1_dram": np.ascontiguousarray(np.concatenate([up1, down1], axis=2)),
        "weights2_dram": np.ascontiguousarray(np.concatenate([*ups2, down2], axis=2)),
        "router_dram": np.ascontiguousarray(np.asarray(L0_ffn_Wg).reshape(EXPERTS2, KD, P).transpose(2, 1, 0)),
        "consts_dram": consts,
    }
    nc = bacc.Bacc("TRN2", target_bir_lowering=False, num_devices=1)
    ins = [nc.dram_tensor(n, a.shape, mybir.dt.from_np(a.dtype), kind="ExternalInput").ap() for n, a in arrays.items()]
    out = nc.dram_tensor("out_dram", (TOKENS, D), F32, kind="ExternalOutput").ap()
    ffn_moe(nc, *ins, out)
    r = run_bass_kernel_spmd(nc, [arrays], core_ids=[0])
    return r.results[0]["out_dram"].reshape(np.asarray(x).shape)
```

```python
from contextlib import ExitStack

import concourse.bass as bass
from concourse import mybir
from concourse.alu_op_type import AluOpType as ALU

F32 = mybir.dt.float32
F32R = mybir.dt.float32r
I32 = mybir.dt.int32
U32 = mybir.dt.uint32
ACT = mybir.ActivationFunctionType

P = 128
TOKENS, D = 1024, 256
TILES = TOKENS // P
HALF_TILES = TILES // 2
HALF = HALF_TILES * P
KD = D // P
VOCAB, EXPERTS1, FF1 = 12500, 4, 256
EXPERTS2, FF2 = 8, 176
CHUNKS = (EXPERTS1 * FF1 // P, EXPERTS2 * FF2 // P)
ROWS = (P // EXPERTS1, P // EXPERTS2)
UPS = (1, 2)
UP_COLS = tuple(n * KD * P for n in UPS)
PIECE = tuple(n + D for n in UP_COLS)
LAG = 2
EPS = 1e-5
RING = 8
WARM = (4, 4)
RSQRT_SEED = 0x5F3759DF - 0x400000 - 2**31
NEWTON_STEPS = 3
PER_EXPERT = VOCAB // EXPERTS1

STEPS = [(b, h, c) for b in range(2) for h in range(2) for c in range(CHUNKS[b])]
FIRST = {(b, h): STEPS.index((b, h, 0)) for b in range(2) for h in range(2)}
LAST = {(b, h): FIRST[b, h] + CHUNKS[b] - 1 for b in range(2) for h in range(2)}
NSTEPS = len(STEPS)

SPLIT_AT = {q: (0, q + 2) for q in range(CHUNKS[0] - 2)}
SPLIT_AT |= {FIRST[0, 1] + 2 * c: (1, c) for c in range(4)}
SPLIT_AT |= {FIRST[1, 0] + c - 4: (1, c) for c in range(4, CHUNKS[1])}

C_IDENT, C_IOTA = 0, P
CONSTS = P + EXPERTS2


def ffn_moe(nc, x, token_ids, weights1, weights2, router, consts, out):
    x_v = x.rearrange("(p t) d -> p t d", t=TILES)
    out_v = out.rearrange("(p t) d -> p t d", t=TILES)

    ctx = ExitStack()
    with ctx:
        def sb(name, shape, dt=F32):
            return ctx.enter_context(nc.sbuf_tensor(name, shape, dt))

        def sem(name):
            return ctx.enter_context(nc.semaphore(name))

        x_sb = sb("x_sb", [P, TILES, D])
        x2_sb = sb("x2_sb", [P, TILES, D])
        norm = sb("norm", [P, HALF_TILES, D])
        out_sb = x_sb
        ids_sb = sb("ids_sb", [P, TILES], I32)
        consts_sb = sb("consts_sb", [P, CONSTS])
        router_raw = sb("router_raw", [P, KD, EXPERTS2])
        router_hl = sb("router_hl", [P, KD, 2, EXPERTS2], F32R)
        raw = sb("raw", [P, RING, PIECE[1]])
        w_hi = (sb("w_hi1", [P, CHUNKS[0], PIECE[0]], F32R), sb("w_hi2", [P, CHUNKS[1], PIECE[1]], F32R))
        w_lo = (sb("w_lo1", [P, CHUNKS[0], PIECE[0]], F32R), sb("w_lo2", [P, CHUNKS[1], PIECE[1]], F32R))
        hT_hi = sb("hT_hi", [P, 2, KD, HALF], F32R)
        hT_lo = sb("hT_lo", [P, 2, KD, HALF], F32R)
        gate = sb("gate", [P, 2, HALF])
        gate_rows = sb("gate_rows", [P, TILES, P])
        silu = sb("silu", [P, 2, HALF])
        gated = sb("gated", [P, 2, HALF])
        act = sb("act", [P, 2, HALF])
        act_hi = sb("act_hi", [P, 2, HALF], F32R)
        act_lo = sb("act_lo", [P, 2, HALF], F32R)
        reached = sb("reached", [P, EXPERTS1 + 1, TILES])
        one_hot = sb("one_hot", [P, EXPERTS1, TILES])
        stats = sb("stats", [P, TILES, 6])
        mv = sb("mv", [P, HALF_TILES, 2])
        var = sb("var", [P, HALF_TILES])
        seed = sb("seed", [P, HALF_TILES], I32)
        rstd = sb("rstd", [P, HALF_TILES])
        newton = sb("newton", [P, HALF_TILES])
        score_part = sb("score_part", [P, HALF_TILES, EXPERTS2])
        score = sb("score", [P, HALF_TILES, EXPERTS2])
        top = sb("top", [P, HALF_TILES, 8])
        top_i = sb("top_i", [P, HALF_TILES, 8], U32)
        gap = sb("gap", [P, HALF_TILES])
        th = sb("th", [P, HALF_TILES])
        prob = sb("prob", [P, 2, HALF_TILES])
        pick = sb("pick", [P, 2, HALF_TILES, EXPERTS2])
        w_tok = sb("w_tok", [P, HALF_TILES, EXPERTS2])

        z = [ctx.enter_context(nc.psum_tensor(f"z{i}", [P, HALF], F32)) for i in range(4)]
        y = [[ctx.enter_context(nc.psum_tensor(f"y{h}{i}", [P, 2 * D], F32)) for i in range(2)] for h in range(2)]

        x_in = [sem(f"x_in{i}") for i in range(TILES // 2)]
        ids_in, consts_in, router_in = sem("ids_in"), sem("consts_in"), sem("router_in")
        w_in = [[sem(f"w_in{b}_{c}") for c in range(CHUNKS[b])] for b in range(2)]
        w_hi_done, w_lo_pool, w_lo_vector = sem("w_hi_done"), sem("w_lo_pool"), sem("w_lo_vector")
        router_split = sem("router_split")
        pool_chain, dve_chain = sem("pool_chain"), sem("dve_chain")
        gate_rows_done = sem("gate_rows_done")
        gate_T, gate_done = sem("gate_T"), sem("gate_done")
        norm_done, norm_T, hT_hi_done, hT_lo_done = sem("norm_done"), sem("norm_T"), sem("hT_hi_done"), sem("hT_lo_done")
        scored, gap_done, th_done = sem("scored"), sem("gap_done"), sem("th_done")
        up_done, silu_done, gated_done, act_done = sem("up_done"), sem("silu_done"), sem("gated_done"), sem("act_done")
        act_hi_done, act_lo_done, down_done = sem("act_hi_done"), sem("act_lo_done"), sem("down_done")
        y_read, out_ready, stored = sem("y_read"), sem("out_ready"), sem("stored")

        block = ctx.enter_context(nc.Block())

        ident = consts_sb[:, C_IDENT:C_IDENT + P]
        iota = consts_sb[:, C_IOTA:C_IOTA + EXPERTS2]

        def piece_no(b, c):
            return b * CHUNKS[0] + c + 1

        def lo_by_vector(b, c):
            return b == 0 and c % 2 == 1

        def wait_lo(engine, b, c):
            if lo_by_vector(b, c):
                engine.wait_ge(w_lo_vector, c // 2 + 1)
            elif b == 0:
                engine.wait_ge(w_lo_pool, c // 2 + 1)
            else:
                engine.wait_ge(w_lo_pool, CHUNKS[0] // 2 + c + 1)

        def raw_piece(b, c):
            return raw[:, (piece_no(b, c) - 1) % RING, 0:PIECE[b]]

        def ln_no(b, h):
            return 2 * b + h

        def gate_bank(b, h):
            return y[1][h] if b == 0 else y[h][0]

        def tiles_of(h):
            return range(h * HALF_TILES, (h + 1) * HALF_TILES)

        @block.sync
        def _(sp):
            def load_piece(b, c):
                if piece_no(b, c) > RING:
                    n = piece_no(b, c) - RING - 1
                    wait_lo(sp, *((0, n) if n < CHUNKS[0] else (1, n - CHUNKS[0])))
                sp.dma_start(raw_piece(b, c), (weights1, weights2)[b][:, c, :]).then_inc(w_in[b][c], 16)

            def load_x(i):
                sp.dma_start(x_sb[:, 2 * i:2 * i + 2, :], x_v[:, 2 * i:2 * i + 2, :]).then_inc(x_in[i], 16)

            load_x(0)
            load_x(1)
            sp.dma_start(consts_sb[:], consts).then_inc(consts_in, 16)
            sp.dma_start(ids_sb[:], token_ids).then_inc(ids_in, 16)
            for c in range(3):
                load_piece(0, c)
            load_x(2)
            load_x(3)
            for c in range(3, CHUNKS[0]):
                load_piece(0, c)
            sp.dma_start(router_raw[:], router).then_inc(router_in, 16)
            for c in range(CHUNKS[1]):
                load_piece(1, c)
            for n in range(4):
                sp.wait_ge(out_ready, n + 1)
                sp.dma_start(out_v[:, 2 * n:2 * n + 2, :], out_sb[:, 2 * n:2 * n + 2, :]).then_inc(stored, 16)
            sp.wait_ge(stored, 64)

        @block.gpsimd
        def _(pool):
            def weight_lo(b, c):
                pool.wait_ge(w_hi_done, piece_no(b, c))
                nc.gpsimd.tensor_tensor(w_lo[b][:, c, :], raw_piece(b, c), w_hi[b][:, c, :].bitcast(F32),
                                        ALU.subtract).then_inc(w_lo_pool, 1)

            nc.gpsimd.memset(reached[:, 0, :], 1.0).then_inc(pool_chain, 1)
            nc.gpsimd.memset(reached[:, EXPERTS1, :], 0.0).then_inc(pool_chain, 1)
            pool.wait_ge(ids_in, 16)
            for e in range(1, EXPERTS1):
                nc.gpsimd.tensor_scalar(reached[:, e, :], ids_sb[:], float(e * PER_EXPERT), None, ALU.is_ge)\
                    .then_inc(pool_chain, 1)
            pool.wait_ge(pool_chain, EXPERTS1 + 1)
            nc.gpsimd.tensor_tensor(one_hot[:], reached[:, 0:EXPERTS1, :], reached[:, 1:, :], ALU.subtract)\
                .then_inc(pool_chain, 1)
            weight_lo(0, 0)
            pool.wait_ge(pool_chain, EXPERTS1 + 2)
            for h in range(2):
                t0 = h * HALF_TILES
                rows = gate_rows[:, t0:t0 + HALF_TILES, :].rearrange("p t (e r) -> p t e r", r=ROWS[0])
                picks = one_hot[:, :, t0:t0 + HALF_TILES].rearrange("p e t -> p t e").unsqueeze(3)
                nc.gpsimd.tensor_copy(rows, picks.to_broadcast([P, HALF_TILES, EXPERTS1, ROWS[0]]))\
                    .then_inc(gate_rows_done, 1)
            for q, (b, h, c) in enumerate(STEPS):
                if b == 0:
                    pool.wait_ge(silu_done, q + 1)
                    if q >= 2:
                        pool.wait_ge(act_done, q - 1)
                    if c == 0:
                        pool.wait_ge(gate_done, ln_no(b, h) + 1)
                    nc.gpsimd.tensor_tensor(gated[:, q % 2, :], silu[:, q % 2, :], gate[:, h, :], ALU.mult)\
                        .then_inc(gated_done, 1)
                if q in SPLIT_AT and not lo_by_vector(*SPLIT_AT[q]):
                    weight_lo(*SPLIT_AT[q])

        @block.scalar
        def _(act_e):
            def weight_hi(b, c):
                act_e.wait_ge(w_in[b][c], 16)
                nc.scalar.copy(w_hi[b][:, c, :], raw_piece(b, c)).then_inc(w_hi_done, 1)

            def tokens_hi(b, h):
                for k in range(KD):
                    act_e.wait_ge(norm_T, KD * ln_no(b, h) + k + 1)
                    if b == 1 and k == 0:
                        act_e.wait_ge(up_done, LAST[0, h] + 1)
                    nc.scalar.copy(hT_hi[:, h, k, :], y[h][k][:]).then_inc(hT_hi_done, 1)

            def gates_out(b, h):
                act_e.wait_ge(gate_T, ln_no(b, h) + 1)
                if b == 1:
                    act_e.wait_ge(gated_done, LAST[0, h] + 1)
                nc.scalar.copy(gate[:, h, :], gate_bank(b, h)[:]).then_inc(gate_done, 1)

            def round_act(q):
                act_e.wait_ge(act_done, q + 1)
                if q >= 2:
                    act_e.wait_ge(down_done, q - 1)
                nc.scalar.copy(act_hi[:, q % 2, :], act[:, q % 2, :]).then_inc(act_hi_done, 1)

            nc.scalar.preload_act_table(ACT.Silu)
            weight_hi(0, 0)
            weight_hi(0, 1)
            tokens_hi(0, 0)
            gates_out(0, 0)
            gates_out(0, 1)
            for q, (b, h, c) in enumerate(STEPS):
                act_e.wait_ge(up_done, q + 1)
                if q >= 2:
                    act_e.wait_ge(act_done, q - 1)
                nc.scalar.activation(silu[:, q % 2, :], z[2 * (q % 2)][:], ACT.Silu).then_inc(silu_done, 1)
                if q >= 1:
                    round_act(q - 1)
                if (b, h, c) == (0, 0, 3):
                    act_e.wait_ge(router_in, 16)
                    nc.scalar.copy(router_hl[:, :, 0, :], router_raw[:]).then_inc(router_split, 1)
                if (b, h, c) == (0, 0, 4):
                    tokens_hi(0, 1)
                for hh in range(2):
                    q0 = LAST[0, hh] + 1
                    if q == q0 + 5:
                        tokens_hi(1, hh)
                    if q == q0 + 6:
                        act_e.wait_ge(gap_done, hh + 1)
                        nc.scalar.activation(th[:], gap[:], ACT.Tanh, scale=0.5).then_inc(th_done, 1)
                    if q == q0 + 8:
                        gates_out(1, hh)
                if q in SPLIT_AT:
                    weight_hi(*SPLIT_AT[q])
            round_act(NSTEPS - 1)

        @block.vector
        def _(dve):
            chain = [0]

            def link(ins):
                chain[0] += 1
                ins.then_inc(dve_chain, 1)
                dve.wait_ge(dve_chain, chain[0])

            def statistics(h, src):
                tiles = tiles_of(h)
                for t in tiles:
                    if src is x_sb and t % 2 == 0:
                        dve.wait_ge(x_in[t // 2], 16)
                    last = nc.vector.bn_stats(stats[:, t, :], src[:, t, :])
                link(last)
                for i, t in enumerate(tiles):
                    last = nc.vector.bn_aggr(mv[:, i, :], stats[:, t, :])
                link(last)

            def inverse_deviation():
                link(nc.vector.tensor_scalar(var[:], mv[:, :, 1], EPS, 0.5, ALU.add, ALU.mult))
                link(nc.vector.tensor_scalar(seed[:], var[:].bitcast(I32), 1, None, ALU.logical_shift_right))
                link(nc.vector.tensor_scalar(rstd[:].bitcast(I32), seed[:], -1.0, float(RSQRT_SEED), ALU.mult, ALU.add))
                for _ in range(NEWTON_STEPS):
                    link(nc.vector.tensor_tensor(newton[:], rstd[:], rstd[:], ALU.mult))
                    link(nc.vector.tensor_tensor(newton[:], newton[:], var[:], ALU.mult))
                    link(nc.vector.scalar_tensor_tensor(rstd[:], newton[:], 1.5, rstd[:], ALU.subtract, ALU.mult))

            def normalise(b, h, src):
                if ln_no(b, h):
                    dve.wait_ge(norm_T, KD * ln_no(b, h))
                for i, t in enumerate(tiles_of(h)):
                    nc.vector.tensor_scalar(norm[:, i, :], src[:, t, :], mv[:, i, 0:1], rstd[:, i:i + 1],
                                            ALU.subtract, ALU.mult).then_inc(norm_done, 1)

            def tokens_lo(b, h):
                for k in range(KD):
                    dve.wait_ge(hT_hi_done, KD * ln_no(b, h) + k + 1)
                    nc.vector.tensor_tensor(hT_lo[:, h, k, :], y[h][k][:], hT_hi[:, h, k, :].bitcast(F32),
                                            ALU.subtract).then_inc(hT_lo_done, 1)

            def add_block(b, h, src, dst, done):
                dve.wait_ge(down_done, LAST[b, h] + 1)
                for i in range(2):
                    t = h * HALF_TILES + 2 * i
                    ins = nc.vector.tensor_tensor(dst[:, t:t + 2, :].rearrange("p t d -> p (t d)"), y[h][i][:],
                                                  src[:, t:t + 2, :].rearrange("p t d -> p (t d)"), ALU.add)
                    ins.then_inc(done, 1)

            def best_two(h):
                dve.wait_ge(scored, h + 1)
                sc = y[h][0][:, 0:HALF_TILES * 2 * EXPERTS2].rearrange("p (t a e) -> p t a e", a=2, e=EXPERTS2)
                link(nc.vector.tensor_copy(score_part[:], sc[:, :, 1, :]))
                link(nc.vector.tensor_tensor(score[:], sc[:, :, 0, :], score_part[:], ALU.add))
                for i in range(HALF_TILES):
                    last = nc.vector.max(top[:, i, :], score[:, i, :])
                link(last)
                for i in range(HALF_TILES):
                    last = nc.vector.max_index(top_i[:, i, :], top[:, i, :], score[:, i, :])
                link(last)
                nc.vector.tensor_tensor(gap[:], top[:, :, 1], top[:, :, 0], ALU.subtract).then_inc(gap_done, 1)
                for j in range(2):
                    last = nc.vector.tensor_tensor(
                        pick[:, j, :, :], iota.unsqueeze(1).to_broadcast([P, HALF_TILES, EXPERTS2]),
                        top_i[:, :, j:j + 1].to_broadcast([P, HALF_TILES, EXPERTS2]), ALU.is_equal)
                link(last)

            def softmax_gates(h):
                dve.wait_ge(th_done, h + 1)
                for j, s in enumerate((-0.5, 0.5)):
                    last = nc.vector.tensor_scalar(prob[:, j, :], th[:], s, 0.5, ALU.mult, ALU.add)
                link(last)
                for j in range(2):
                    last = nc.vector.tensor_tensor(
                        pick[:, j, :, :], pick[:, j, :, :],
                        prob[:, j, :].unsqueeze(2).to_broadcast([P, HALF_TILES, EXPERTS2]), ALU.mult)
                link(last)
                link(nc.vector.tensor_tensor(w_tok[:], pick[:, 0, :, :], pick[:, 1, :, :], ALU.add))
                for i, t in enumerate(tiles_of(h)):
                    nc.vector.tensor_copy(gate_rows[:, t, :].rearrange("p (e r) -> p e r", r=ROWS[1]),
                                          w_tok[:, i, :].unsqueeze(2).to_broadcast([P, EXPERTS2, ROWS[1]]))\
                        .then_inc(gate_rows_done, 1)

            def act_low(q):
                dve.wait_ge(act_hi_done, q + 1)
                if q >= 2:
                    dve.wait_ge(down_done, q - 1)
                nc.vector.tensor_tensor(act_lo[:, q % 2, :], act[:, q % 2, :], act_hi[:, q % 2, :].bitcast(F32),
                                        ALU.subtract).then_inc(act_lo_done, 1)

            def weight_lo(b, c):
                dve.wait_ge(w_hi_done, piece_no(b, c))
                nc.vector.tensor_tensor(w_lo[b][:, c, :], raw_piece(b, c), w_hi[b][:, c, :].bitcast(F32),
                                        ALU.subtract).then_inc(w_lo_vector, 1)

            statistics(0, x_sb)
            inverse_deviation()
            normalise(0, 0, x_sb)
            tokens_lo(0, 0)
            weight_lo(0, 1)
            for q, (b, h, c) in enumerate(STEPS):
                if b == 1:
                    dve.wait_ge(up_done, q + 1)
                    if c == 0:
                        dve.wait_ge(gate_done, ln_no(b, h) + 1)
                    nc.vector.tensor_tensor(gated[:, q % 2, :], gate[:, h, :], z[2 * (q % 2) + 1][:], ALU.mult)\
                        .then_inc(gated_done, 1)
                if q >= 1:
                    act_low(q - 1)
                dve.wait_ge(gated_done, q + 1)
                if b == 0:
                    nc.vector.tensor_tensor(act[:, q % 2, :], gated[:, q % 2, :], z[2 * (q % 2)][:], ALU.mult)\
                        .then_inc(act_done, 1)
                else:
                    dve.wait_ge(silu_done, q + 1)
                    nc.vector.tensor_tensor(act[:, q % 2, :], gated[:, q % 2, :], silu[:, q % 2, :], ALU.mult)\
                        .then_inc(act_done, 1)
                if q in SPLIT_AT and lo_by_vector(*SPLIT_AT[q]):
                    weight_lo(*SPLIT_AT[q])
                if q == 3:
                    dve.wait_ge(router_split, 1)
                    nc.vector.tensor_tensor(router_hl[:, :, 1, :], router_raw[:], router_hl[:, :, 0, :].bitcast(F32),
                                            ALU.subtract).then_inc(router_split, 1)
                if q == 1:
                    statistics(1, x_sb)
                if q == 2:
                    inverse_deviation()
                if q == 3:
                    normalise(0, 1, x_sb)
                if q == 4:
                    tokens_lo(0, 1)
                for hh in range(2):
                    q0 = LAST[0, hh] + 1
                    if q == q0 + 2:
                        add_block(0, hh, x_sb, x2_sb, y_read)
                    if q == q0 + 3:
                        dve.wait_ge(y_read, 2 * hh + 2)
                        statistics(hh, x2_sb)
                    if q == q0 + 4:
                        inverse_deviation()
                        normalise(1, hh, x2_sb)
                    if q == q0 + 5:
                        tokens_lo(1, hh)
                    if q == q0 + 6:
                        best_two(hh)
                    if q == q0 + 7:
                        softmax_gates(hh)
                if q == LAST[1, 0] + 3:
                    add_block(1, 0, x2_sb, out_sb, out_ready)
            act_low(NSTEPS - 1)
            add_block(1, 1, x2_sb, out_sb, out_ready)

        @block.tensor
        def _(pe):
            def transpose_gates(b, h, bank):
                for i, t in enumerate(tiles_of(h)):
                    pe.wait_ge(gate_rows_done, h + 1 if b == 0 else 2 + t + 1)
                    last = nc.tensor.transpose(bank[:, i * P:(i + 1) * P], gate_rows[:, t, :], ident)
                last.then_inc(gate_T, 1)

            def transpose_tokens(b, h):
                for k in range(KD):
                    for i in range(HALF_TILES):
                        pe.wait_ge(norm_done, HALF_TILES * ln_no(b, h) + i + 1)
                        last = nc.tensor.transpose(y[h][k][:, i * P:(i + 1) * P], norm[:, i, k * P:(k + 1) * P], ident)
                    last.then_inc(norm_T, 1)

            def route_scores(h):
                pe.wait_ge(hT_lo_done, KD * ln_no(1, h) + KD)
                pe.wait_ge(router_split, 2)
                for i in range(HALF_TILES):
                    cols = slice(i * P, (i + 1) * P)
                    o = y[h][0][:, i * 2 * EXPERTS2:(i + 1) * 2 * EXPERTS2]
                    for j, k in enumerate((0, 1)):
                        if k == KD - 1:
                            for kk in range(KD):
                                nc.tensor.matmul(o[:, 0:EXPERTS2], hT_lo[:, h, kk, cols], router_hl[:, kk, 0, :],
                                                 start=False, stop=False)
                        last = nc.tensor.matmul(o, hT_hi[:, h, k, cols],
                                                router_hl[:, k, :, :].rearrange("p a e -> p (a e)"),
                                                start=(k == 0), stop=(k == KD - 1))
                last.then_inc(scored, 1)

            def up(q):
                b, h, c = STEPS[q]
                wait_lo(pe, b, c)
                if c == 0:
                    pe.wait_ge(hT_lo_done, KD * ln_no(b, h) + KD)
                if q >= 2:
                    pe.wait_ge(act_done, q - 1)
                for m in range(UPS[b]):
                    bank = z[2 * (q % 2) + m]
                    for k in range(KD):
                        cols = slice((m * KD + k) * P, (m * KD + k + 1) * P)
                        nc.tensor.matmul(bank[:], w_lo[b][:, c, cols], hT_hi[:, h, k, :], start=(k == 0), stop=False)
                        nc.tensor.matmul(bank[:], w_hi[b][:, c, cols], hT_lo[:, h, k, :], start=False, stop=False)
                        last = nc.tensor.matmul(bank[:], w_hi[b][:, c, cols], hT_hi[:, h, k, :], start=False,
                                                stop=(k == KD - 1))
                last.then_inc(up_done, 1)

            def down(q):
                b, h, c = STEPS[q]
                pe.wait_ge(act_lo_done, q + 1)
                wd = slice(UP_COLS[b], PIECE[b])
                for i in range(HALF_TILES):
                    rows = slice(i * P, (i + 1) * P)
                    o = y[h][i // 2][:, (i % 2) * D:(i % 2 + 1) * D]
                    first = c == 0 and i % 2 == 0
                    for j, (a, w) in enumerate(((act_lo, w_hi), (act_hi, w_lo), (act_hi, w_hi))):
                        last = nc.tensor.matmul(o, a[:, q % 2, rows], w[b][:, c, wd], start=(first and j == 0),
                                                stop=(c == CHUNKS[b] - 1 and j == 2), skip_group_check=True)
                last.then_inc(down_done, 1)

            def warm(n):
                pe.wait_ge(w_hi_done, 1)
                for _ in range(n):
                    nc.tensor.matmul(z[3][:], w_hi[0][:, 0, 0:P], w_hi[0][:, 0, 0:HALF], start=True, stop=True)

            pe.wait_ge(consts_in, 16)
            warm(WARM[0])
            transpose_tokens(0, 0)
            warm(WARM[1])
            transpose_gates(0, 0, gate_bank(0, 0))
            for q in range(NSTEPS + LAG):
                if q < NSTEPS:
                    up(q)
                if q == 0:
                    transpose_gates(0, 1, gate_bank(0, 1))
                if q == 4:
                    pe.wait_ge(gate_done, 2)
                    transpose_tokens(0, 1)
                for hh in range(2):
                    q0 = LAST[0, hh] + 1
                    if q == q0 + 5:
                        pe.wait_ge(y_read, 2 * hh + 2)
                        transpose_tokens(1, hh)
                    if q == q0 + 6:
                        route_scores(hh)
                    if q == q0 + 8:
                        transpose_gates(1, hh, gate_bank(1, hh))
                if q >= LAG:
                    b, h, c = STEPS[q - LAG]
                    if c == 0:
                        if b == 0:
                            pe.wait_ge(hT_lo_done, KD * ln_no(0, h) + KD)
                        else:
                            pe.wait_ge(gate_done, ln_no(1, h) + 1)
                    down(q - LAG)


def kernel(x, itok_BxS_13_99985, ctx_2048, L0_ffn_Wg, L0_ffn_W1, L0_ffn_W2, L0_ffn_W3):
    import numpy as np
    import concourse.bacc as bacc
    from concourse.bass_utils import run_bass_kernel_spmd

    c1, c2 = CHUNKS
    ctx = np.asarray(ctx_2048)
    up1 = ctx.reshape(EXPERTS1, c1, ROWS[0], KD, P).transpose(4, 1, 3, 0, 2).reshape(P, c1, KD * P)
    down1 = ctx.reshape(EXPERTS1, D, c1, ROWS[0]).transpose(0, 3, 2, 1).reshape(P, c1, D)
    ups2 = [np.asarray(w).reshape(EXPERTS2, c2, ROWS[1], KD, P).transpose(4, 1, 3, 0, 2).reshape(P, c2, KD * P)
            for w in (L0_ffn_W1, L0_ffn_W2)]
    down2 = np.asarray(L0_ffn_W3).reshape(EXPERTS2, D, c2, ROWS[1]).transpose(0, 3, 2, 1).reshape(P, c2, D)
    consts = np.zeros((P, CONSTS), np.float32)
    consts[:, C_IDENT:C_IDENT + P] = np.eye(P)
    consts[:, C_IOTA:] = np.arange(EXPERTS2)
    arrays = {
        "x_dram": np.ascontiguousarray(np.asarray(x).reshape(TOKENS, D)),
        "token_ids_dram": np.ascontiguousarray(np.asarray(itok_BxS_13_99985).reshape(P, TILES)),
        "weights1_dram": np.ascontiguousarray(np.concatenate([up1, down1], axis=2)),
        "weights2_dram": np.ascontiguousarray(np.concatenate([*ups2, down2], axis=2)),
        "router_dram": np.ascontiguousarray(np.asarray(L0_ffn_Wg).reshape(EXPERTS2, KD, P).transpose(2, 1, 0)),
        "consts_dram": consts,
    }
    nc = bacc.Bacc("TRN2", target_bir_lowering=False, num_devices=1)
    ins = [nc.dram_tensor(n, a.shape, mybir.dt.from_np(a.dtype), kind="ExternalInput").ap() for n, a in arrays.items()]
    out = nc.dram_tensor("out_dram", (TOKENS, D), F32, kind="ExternalOutput").ap()
    ffn_moe(nc, *ins, out)
    r = run_bass_kernel_spmd(nc, [arrays], core_ids=[0])
    return r.results[0]["out_dram"].reshape(np.asarray(x).shape)
```

```python
from contextlib import ExitStack

import concourse.bass as bass
from concourse import mybir
from concourse.alu_op_type import AluOpType as ALU

F32 = mybir.dt.float32
F32R = mybir.dt.float32r
I32 = mybir.dt.int32
U32 = mybir.dt.uint32
ACT = mybir.ActivationFunctionType

P = 128
TOKENS, D = 1024, 256
TILES = TOKENS // P
HALF_TILES = TILES // 2
HALF = HALF_TILES * P
KD = D // P
VOCAB, EXPERTS1, FF1 = 12500, 4, 256
EXPERTS2, FF2 = 8, 176
CHUNKS = (EXPERTS1 * FF1 // P, EXPERTS2 * FF2 // P)
ROWS = (P // EXPERTS1, P // EXPERTS2)
UPS = (1, 2)
UP_COLS = tuple(n * KD * P for n in UPS)
PIECE = tuple(n + D for n in UP_COLS)
EPS = 1e-5
PER_EXPERT = VOCAB // EXPERTS1

LAG = 3
BUFFERS = 3
RING = 5
WARM = 12

STEPS = [(b, h, c) for b in range(2) for h in range(2) for c in range(CHUNKS[b])]
FIRST = {(b, h): STEPS.index((b, h, 0)) for b in range(2) for h in range(2)}
LAST = {(b, h): FIRST[b, h] + CHUNKS[b] - 1 for b in range(2) for h in range(2)}
NSTEPS = len(STEPS)

WAYS = ((0, 1), (1, 0), (1, 1))
WAY_START = {(0, 1): 0, (1, 0): LAST[0, 0] + 1, (1, 1): LAST[0, 1] + 1}
STAGES = {
    "sum": (None, 1, 2),
    "statistics": (None, 3, 3),
    "inverse_deviation": (1, 4, 5),
    "normalise": (1, 4, 4),
    "transpose_tokens": ((4, 0), (6, 0), (6, 1)),
    "tokens_hi": (4, 5, 6),
    "tokens_lo": (5, 5, 6),
    "scores": (None, (7, 0), (7, 0)),
    "score_rows": (None, 7, 7),
    "transpose_scores": (None, (7, 1), (7, 1)),
    "best_two": (None, 7, 8),
    "tanh": (None, 7, 8),
    "softmax": (None, 7, 8),
    "transpose_gates": ((3, 0), (8, 1), (10, 1)),
    "gates_out": (2, 8, 9),
}

FIRST_PIECES = 4
SPLIT_AT = {c - 3: (0, c) for c in range(FIRST_PIECES, CHUNKS[0])}
SPLIT_AT |= {5 + 2 * c: (1, c) for c in range(4)}
SPLIT_AT |= {FIRST[1, 0] + c - 4: (1, c) for c in range(4, CHUNKS[1])}
VECTOR_LO = ((0, 0), (0, 5), (0, 7))
ROUTER_STEP = 3


def due(stage, q, slot=None):
    found = []
    for way, at in zip(WAYS, STAGES[stage]):
        if at is not None and at == ((q - WAY_START[way]) if slot is None else (q - WAY_START[way], slot)):
            found.append(way)
    return found


C_IDENT, C_IOTA = 0, P
CONSTS = P + EXPERTS2


def ffn_moe(nc, x, token_ids, weights1, weights2, router, consts, out):
    x_v = x.rearrange("(p t) d -> p t d", t=TILES)
    out_v = out.rearrange("(p t) d -> p t d", t=TILES)

    ctx = ExitStack()
    with ctx:
        def sb(name, shape, dt=F32):
            return ctx.enter_context(nc.sbuf_tensor(name, shape, dt))

        def sem(name):
            return ctx.enter_context(nc.semaphore(name))

        x_sb = sb("x_sb", [P, TILES, D])
        x2_sb = sb("x2_sb", [P, TILES, D])
        norm = sb("norm", [P, HALF_TILES, D])
        out_sb = x_sb
        ids_sb = sb("ids_sb", [P, TILES], I32)
        consts_sb = sb("consts_sb", [P, CONSTS])
        router_raw = sb("router_raw", [P, KD, EXPERTS2])
        router_hl = sb("router_hl", [P, KD, 2, EXPERTS2], F32R)
        raw = sb("raw", [P, RING, PIECE[1]])
        warm_sb = sb("warm_sb", [P, HALF], mybir.dt.bfloat16)
        w_hi = (sb("w_hi1", [P, CHUNKS[0], PIECE[0]], F32R), sb("w_hi2", [P, CHUNKS[1], PIECE[1]], F32R))
        w_lo = (sb("w_lo1", [P, CHUNKS[0], PIECE[0]], F32R), sb("w_lo2", [P, CHUNKS[1], PIECE[1]], F32R))
        hT_hi = sb("hT_hi", [P, 2, KD, HALF], F32R)
        hT_lo = sb("hT_lo", [P, 2, KD, HALF], F32R)
        gate = sb("gate", [P, 2, HALF])
        gate_rows = sb("gate_rows", [P, TILES, P])
        silu = sb("silu", [P, BUFFERS, HALF])
        gated = sb("gated", [P, BUFFERS, HALF])
        act = sb("act", [P, BUFFERS, HALF])
        act_hi = sb("act_hi", [P, BUFFERS, HALF], F32R)
        act_lo = sb("act_lo", [P, BUFFERS, HALF], F32R)
        reached = sb("reached", [P, EXPERTS1 + 1, TILES])
        one_hot = sb("one_hot", [P, EXPERTS1, TILES])
        stats = sb("stats", [P, TILES, 6])
        mv = sb("mv", [P, TILES, 2])
        var = sb("var", [P, TILES])
        rstd = sb("rstd", [P, TILES])
        minus_half = sb("minus_half", [P, HALF_TILES])
        score_part = sb("score_part", [P, HALF_TILES, EXPERTS2])
        score = sb("score", [P, HALF_TILES, EXPERTS2])
        top = sb("top", [P, HALF_TILES, 8])
        top_i = sb("top_i", [P, HALF_TILES, 8], U32)
        score_rows = sb("score_rows", [2 * EXPERTS2, HALF])
        gap = sb("gap", [P, HALF_TILES])
        th = sb("th", [P, HALF_TILES])
        prob = sb("prob", [P, 2, HALF_TILES])
        pick = sb("pick", [P, 2, HALF_TILES, EXPERTS2])
        w_tok = sb("w_tok", [P, HALF_TILES, EXPERTS2])

        z = [ctx.enter_context(nc.psum_tensor(f"z{i}", [P, HALF], F32)) for i in range(4)]
        y = [[ctx.enter_context(nc.psum_tensor(f"y{h}{i}", [P, 2 * D], F32)) for i in range(2)] for h in range(2)]

        x_in = [sem(f"x_in{i}") for i in range(TILES // 2)]
        ids_in, consts_in, router_in = sem("ids_in"), sem("consts_in"), sem("router_in")
        w_in = [[sem(f"w_in{b}_{c}") for c in range(CHUNKS[b])] for b in range(2)]
        w_hi_done, w_lo_pool, w_lo_vector = sem("w_hi_done"), sem("w_lo_pool"), sem("w_lo_vector")
        router_hi_done, router_lo_done = sem("router_hi_done"), sem("router_lo_done")
        reached_done, one_hot_done, gate_rows_done = sem("reached_done"), sem("one_hot_done"), sem("gate_rows_done")
        gate_T, gate_done = sem("gate_T"), sem("gate_done")
        var_done, rstd_done = sem("var_done"), sem("rstd_done")
        norm_done, norm_T, hT_hi_done, hT_lo_done = sem("norm_done"), sem("norm_T"), sem("hT_hi_done"), sem("hT_lo_done")
        scored, score_rows_done, scores_T = sem("scored"), sem("score_rows_done"), sem("scores_T")
        gap_done, th_done = sem("gap_done"), sem("th_done")
        up_done, silu_done, gated_done, act_done = sem("up_done"), sem("silu_done"), sem("gated_done"), sem("act_done")
        act_hi_done, act_lo_done = sem("act_hi_done"), sem("act_lo_done")
        down_done, last_first_bank = sem("down_done"), sem("last_first_bank")
        warm_in, x2_done, out_ready, stored = sem("warm_in"), sem("x2_done"), sem("out_ready"), sem("stored")
        vector_chain = sem("vector_chain")

        block = ctx.enter_context(nc.Block())

        ident = consts_sb[:, C_IDENT:C_IDENT + P]
        iota = consts_sb[:, C_IOTA:C_IOTA + EXPERTS2]

        def piece_no(b, c):
            return b * CHUNKS[0] + c + 1

        def wait_lo(engine, b, c):
            vector = [p for p in VECTOR_LO if p <= (b, c)]
            if (b, c) in VECTOR_LO:
                engine.wait_ge(w_lo_vector, len(vector))
            else:
                engine.wait_ge(w_lo_pool, piece_no(b, c) - len(vector))

        def raw_piece(b, c):
            return raw[:, (piece_no(b, c) - 1) % RING, 0:PIECE[b]]

        def ln_no(b, h):
            return 2 * b + h

        def gate_bank(b, h):
            return y[1][h] if b == 0 else y[h][0]

        def z_banks(q):
            return [z[q % 4]] if STEPS[q][0] == 0 else z[2 * (q % 2):2 * (q % 2) + 2]

        def tiles_of(h):
            return range(h * HALF_TILES, (h + 1) * HALF_TILES)

        @block.sync
        def _(sp):
            def load_piece(b, c):
                if piece_no(b, c) > RING:
                    n = piece_no(b, c) - RING - 1
                    wait_lo(sp, *((0, n) if n < CHUNKS[0] else (1, n - CHUNKS[0])))
                sp.dma_start(raw_piece(b, c), (weights1, weights2)[b][:, c, :]).then_inc(w_in[b][c], 16)

            def load_x(i):
                sp.dma_start(x_sb[:, 2 * i:2 * i + 2, :], x_v[:, 2 * i:2 * i + 2, :]).then_inc(x_in[i], 16)

            load_x(0)
            load_x(1)
            sp.dma_start(ids_sb[:], token_ids).then_inc(ids_in, 16)
            sp.dma_start(consts_sb[:], consts).then_inc(consts_in, 16)
            for c in range(3):
                load_piece(0, c)
            load_x(2)
            load_x(3)
            for c in range(3, CHUNKS[0]):
                load_piece(0, c)
            sp.dma_start(router_raw[:], router).then_inc(router_in, 16)
            for c in range(CHUNKS[1]):
                load_piece(1, c)
            for pair in range(TILES // 2):
                sp.wait_ge(out_ready, pair + 1)
                sp.dma_start(out_v[:, 2 * pair:2 * pair + 2, :], out_sb[:, 2 * pair:2 * pair + 2, :]).then_inc(stored, 16)
            sp.wait_ge(stored, 16 * (TILES // 2))

        @block.gpsimd
        def _(pool):
            def weight_lo(b, c):
                pool.wait_ge(w_hi_done, piece_no(b, c))
                nc.gpsimd.tensor_tensor(w_lo[b][:, c, :], raw_piece(b, c), w_hi[b][:, c, :].bitcast(F32),
                                        ALU.subtract).then_inc(w_lo_pool, 1)

            def inverse_deviation(b, h):
                pool.wait_ge(var_done, ln_no(b, h) + 1)
                cols = slice(h * HALF_TILES, (h + 1) * HALF_TILES)
                nc.gpsimd.tensor_tensor(rstd[:, cols], var[:, cols], minus_half[:], ALU.pow).then_inc(rstd_done, 1)

            nc.gpsimd.memset(minus_half[:], -0.5).then_inc(reached_done, 1)
            nc.gpsimd.memset(reached[:, 0, :], 1.0).then_inc(reached_done, 1)
            nc.gpsimd.memset(reached[:, EXPERTS1, :], 0.0).then_inc(reached_done, 1)
            pool.wait_ge(ids_in, 16)
            for e in range(1, EXPERTS1):
                nc.gpsimd.tensor_scalar(reached[:, e, :], ids_sb[:], float(e * PER_EXPERT), None, ALU.is_ge)\
                    .then_inc(reached_done, 1)
            pool.wait_ge(reached_done, EXPERTS1 + 2)
            nc.gpsimd.tensor_tensor(one_hot[:], reached[:, 0:EXPERTS1, :], reached[:, 1:, :], ALU.subtract)\
                .then_inc(one_hot_done, 1)
            inverse_deviation(0, 0)
            for c in range(FIRST_PIECES):
                if (0, c) not in VECTOR_LO:
                    weight_lo(0, c)
            for q, (b, h, c) in enumerate(STEPS):
                if b == 0:
                    pool.wait_ge(silu_done, q + 1)
                    if q >= BUFFERS:
                        pool.wait_ge(act_done, q - BUFFERS + 1)
                    if c == 0:
                        pool.wait_ge(gate_done, ln_no(b, h) + 1)
                    nc.gpsimd.tensor_tensor(gated[:, q % BUFFERS, :], silu[:, q % BUFFERS, :], gate[:, h, :], ALU.mult)\
                        .then_inc(gated_done, 1)
                for way in due("inverse_deviation", q):
                    inverse_deviation(*way)
                if q in SPLIT_AT and SPLIT_AT[q] not in VECTOR_LO:
                    weight_lo(*SPLIT_AT[q])

        @block.scalar
        def _(act_e):
            def weight_hi(b, c):
                act_e.wait_ge(w_in[b][c], 16)
                nc.scalar.copy(w_hi[b][:, c, :], raw_piece(b, c)).then_inc(w_hi_done, 1)

            def tokens_hi(b, h):
                for k in range(KD):
                    act_e.wait_ge(norm_T, KD * ln_no(b, h) + k + 1)
                    if b == 1 and k == 0:
                        act_e.wait_ge(up_done, LAST[0, h] + 1)
                    nc.scalar.copy(hT_hi[:, h, k, :], y[h][k][:]).then_inc(hT_hi_done, 1)

            def gates_out(b, h):
                act_e.wait_ge(gate_T, ln_no(b, h) + 1)
                if b == 1:
                    act_e.wait_ge(gated_done, LAST[0, h] + 1)
                nc.scalar.copy(gate[:, h, :], gate_bank(b, h)[:]).then_inc(gate_done, 1)

            def round_act(q):
                act_e.wait_ge(act_done, q + 1)
                if q >= BUFFERS:
                    act_e.wait_ge(down_done, q - BUFFERS + 1)
                nc.scalar.copy(act_hi[:, q % BUFFERS, :], act[:, q % BUFFERS, :]).then_inc(act_hi_done, 1)

            def spread_gates(h):
                t0 = h * HALF_TILES
                rows = gate_rows[:, t0:t0 + HALF_TILES, :].rearrange("p t (e r) -> p t e r", r=ROWS[0])
                picks = one_hot[:, :, t0:t0 + HALF_TILES].rearrange("p e t -> p t e").unsqueeze(3)
                nc.scalar.copy(rows, picks.to_broadcast([P, HALF_TILES, EXPERTS1, ROWS[0]]))\
                    .then_inc(gate_rows_done, 1)

            nc.scalar.preload_act_table(ACT.Silu)
            weight_hi(0, 0)
            act_e.wait_ge(one_hot_done, 1)
            spread_gates(0)
            weight_hi(0, 1)
            weight_hi(0, 2)
            tokens_hi(0, 0)
            weight_hi(0, 3)
            gates_out(0, 0)
            spread_gates(1)
            for q, (b, h, c) in enumerate(STEPS):
                act_e.wait_ge(up_done, q + 1)
                if q >= BUFFERS:
                    act_e.wait_ge(act_done, q - BUFFERS + 1)
                nc.scalar.activation(silu[:, q % BUFFERS, :], z_banks(q)[0][:], ACT.Silu).then_inc(silu_done, 1)
                if q >= 1:
                    round_act(q - 1)
                if q == ROUTER_STEP:
                    act_e.wait_ge(router_in, 16)
                    nc.scalar.copy(router_hl[:, :, 0, :], router_raw[:]).then_inc(router_hi_done, 1)
                for way in due("tokens_hi", q):
                    tokens_hi(*way)
                for _, hh in due("score_rows", q):
                    act_e.wait_ge(scored, hh + 1)
                    nc.scalar.copy(score_rows[:], y[hh][0][0:2 * EXPERTS2, :]).then_inc(score_rows_done, 1)
                for _, hh in due("tanh", q):
                    act_e.wait_ge(gap_done, hh + 1)
                    nc.scalar.activation(th[:], gap[:], ACT.Tanh, scale=0.5).then_inc(th_done, 1)
                for way in due("gates_out", q):
                    gates_out(*way)
                if q in SPLIT_AT:
                    weight_hi(*SPLIT_AT[q])
            round_act(NSTEPS - 1)

        @block.vector
        def _(dve):
            chain = [0]

            def link(ins):
                chain[0] += 1
                ins.then_inc(vector_chain, 1)
                dve.wait_ge(vector_chain, chain[0])

            def statistics(h, src):
                tiles = tiles_of(h)
                for t in tiles:
                    if src is x_sb and t % 2 == 0:
                        dve.wait_ge(x_in[t // 2], 16)
                    last = nc.vector.bn_stats(stats[:, t, :], src[:, t, :])
                link(last)
                for t in tiles:
                    last = nc.vector.bn_aggr(mv[:, t, :], stats[:, t, :])
                link(last)

                cols = slice(h * HALF_TILES, (h + 1) * HALF_TILES)
                nc.vector.tensor_scalar(var[:, cols], mv[:, cols, 1], EPS, None, ALU.add).then_inc(var_done, 1)

            def normalise(b, h, src):
                dve.wait_ge(rstd_done, ln_no(b, h) + 1)
                if ln_no(b, h):
                    dve.wait_ge(norm_T, KD * ln_no(b, h))
                for i, t in enumerate(tiles_of(h)):
                    nc.vector.tensor_scalar(norm[:, i, :], src[:, t, :], mv[:, t, 0:1], rstd[:, t:t + 1],
                                            ALU.subtract, ALU.mult).then_inc(norm_done, 1)

            def tokens_lo(b, h):
                for k in range(KD):
                    dve.wait_ge(hT_hi_done, KD * ln_no(b, h) + k + 1)
                    nc.vector.tensor_tensor(hT_lo[:, h, k, :], y[h][k][:], hT_hi[:, h, k, :].bitcast(F32),
                                            ALU.subtract).then_inc(hT_lo_done, 1)

            def add_bank(h, i, src, dst, done):
                t = h * HALF_TILES + 2 * i
                nc.vector.tensor_tensor(dst[:, t:t + 2, :].rearrange("p t d -> p (t d)"), y[h][i][:],
                                        src[:, t:t + 2, :].rearrange("p t d -> p (t d)"), ALU.add).then_inc(done, 1)

            def add_block(b, h, src, dst, done):
                dve.wait_ge(down_done, LAST[b, h] + 1)
                for i in range(2):
                    add_bank(h, i, src, dst, done)

            def best_two(h):
                dve.wait_ge(scores_T, h + 1)
                sc = y[h][1][:, 0:HALF_TILES * 2 * EXPERTS2].rearrange("p (t a e) -> p t a e", a=2, e=EXPERTS2)
                link(nc.vector.tensor_copy(score_part[:], sc[:, :, 1, :]))
                link(nc.vector.tensor_tensor(score[:], sc[:, :, 0, :], score_part[:], ALU.add))
                for i in range(HALF_TILES):
                    last = nc.vector.max(top[:, i, :], score[:, i, :])
                link(last)
                for i in range(HALF_TILES):
                    last = nc.vector.max_index(top_i[:, i, :], top[:, i, :], score[:, i, :])
                link(last)
                nc.vector.tensor_tensor(gap[:], top[:, :, 1], top[:, :, 0], ALU.subtract).then_inc(gap_done, 1)
                for j in range(2):
                    last = nc.vector.tensor_tensor(
                        pick[:, j, :, :], iota.unsqueeze(1).to_broadcast([P, HALF_TILES, EXPERTS2]),
                        top_i[:, :, j:j + 1].to_broadcast([P, HALF_TILES, EXPERTS2]), ALU.is_equal)
                link(last)

            def softmax_gates(h):
                dve.wait_ge(th_done, h + 1)
                for j, s in enumerate((-0.5, 0.5)):
                    last = nc.vector.tensor_scalar(prob[:, j, :], th[:], s, 0.5, ALU.mult, ALU.add)
                link(last)
                for j in range(2):
                    last = nc.vector.tensor_tensor(
                        pick[:, j, :, :], pick[:, j, :, :],
                        prob[:, j, :].unsqueeze(2).to_broadcast([P, HALF_TILES, EXPERTS2]), ALU.mult)
                link(last)
                link(nc.vector.tensor_tensor(w_tok[:], pick[:, 0, :, :], pick[:, 1, :, :], ALU.add))
                for i, t in enumerate(tiles_of(h)):
                    nc.vector.tensor_copy(gate_rows[:, t, :].rearrange("p (e r) -> p e r", r=ROWS[1]),
                                          w_tok[:, i, :].unsqueeze(2).to_broadcast([P, EXPERTS2, ROWS[1]]))\
                        .then_inc(gate_rows_done, 1)

            def act_low(q):
                dve.wait_ge(act_hi_done, q + 1)
                if q >= BUFFERS:
                    dve.wait_ge(down_done, q - BUFFERS + 1)
                i = q % BUFFERS
                nc.vector.tensor_tensor(act_lo[:, i, :], act[:, i, :], act_hi[:, i, :].bitcast(F32), ALU.subtract)\
                    .then_inc(act_lo_done, 1)

            def weight_lo(b, c):
                dve.wait_ge(w_hi_done, piece_no(b, c))
                nc.vector.tensor_tensor(w_lo[b][:, c, :], raw_piece(b, c), w_hi[b][:, c, :].bitcast(F32),
                                        ALU.subtract).then_inc(w_lo_vector, 1)

            nc.vector.memset(warm_sb[:], 0.0).then_inc(warm_in, 1)
            statistics(0, x_sb)
            for c in range(FIRST_PIECES):
                if (0, c) in VECTOR_LO:
                    weight_lo(0, c)
            normalise(0, 0, x_sb)
            tokens_lo(0, 0)
            statistics(1, x_sb)
            for q, (b, h, c) in enumerate(STEPS):
                i = q % BUFFERS
                if b == 1:
                    dve.wait_ge(up_done, q + 1)
                    if c == 0:
                        dve.wait_ge(gate_done, ln_no(b, h) + 1)
                    nc.vector.tensor_tensor(gated[:, i, :], gate[:, h, :], z_banks(q)[1][:], ALU.mult)\
                        .then_inc(gated_done, 1)
                if q >= 1:
                    act_low(q - 1)
                dve.wait_ge(gated_done, q + 1)
                if b == 1:
                    dve.wait_ge(silu_done, q + 1)
                factor = z_banks(q)[0][:] if b == 0 else silu[:, i, :]
                nc.vector.tensor_tensor(act[:, i, :], gated[:, i, :], factor, ALU.mult).then_inc(act_done, 1)
                if q in SPLIT_AT and SPLIT_AT[q] in VECTOR_LO:
                    weight_lo(*SPLIT_AT[q])
                if q == ROUTER_STEP:
                    dve.wait_ge(router_hi_done, 1)
                    nc.vector.tensor_tensor(router_hl[:, :, 1, :], router_raw[:], router_hl[:, :, 0, :].bitcast(F32),
                                            ALU.subtract).then_inc(router_lo_done, 1)
                for _, hh in due("sum", q):
                    add_block(0, hh, x_sb, x2_sb, x2_done)
                for _, hh in due("statistics", q):
                    dve.wait_ge(x2_done, 2 * hh + 2)
                    statistics(hh, x2_sb)
                for bb, hh in due("normalise", q):
                    normalise(bb, hh, (x_sb, x2_sb)[bb])
                for way in due("tokens_lo", q):
                    tokens_lo(*way)
                for _, hh in due("best_two", q):
                    best_two(hh)
                for _, hh in due("softmax", q):
                    softmax_gates(hh)
                if q == LAST[1, 0] + LAG + 1:
                    add_block(1, 0, x2_sb, out_sb, out_ready)
            act_low(NSTEPS - 1)
            for i in range(2):
                if i == 0:
                    dve.wait_ge(last_first_bank, 1)
                else:
                    dve.wait_ge(down_done, NSTEPS)
                add_bank(1, i, x2_sb, out_sb, out_ready)

        @block.tensor
        def _(pe):
            def transpose_gates(b, h, bank):
                for i, t in enumerate(tiles_of(h)):
                    pe.wait_ge(gate_rows_done, h + 1 if b == 0 else 2 + t + 1)
                    last = nc.tensor.transpose(bank[:, i * P:(i + 1) * P], gate_rows[:, t, :], ident)
                last.then_inc(gate_T, 1)

            def transpose_tokens(b, h):
                for k in range(KD):
                    for i in range(HALF_TILES):
                        pe.wait_ge(norm_done, HALF_TILES * ln_no(b, h) + i + 1)
                        last = nc.tensor.transpose(y[h][k][:, i * P:(i + 1) * P], norm[:, i, k * P:(k + 1) * P], ident)
                    last.then_inc(norm_T, 1)

            def route_scores(h):
                pe.wait_ge(hT_lo_done, KD * ln_no(1, h) + KD)
                pe.wait_ge(router_lo_done, 1)
                for k in range(KD):
                    nc.tensor.matmul(y[h][0][0:2 * EXPERTS2, :], router_hl[:, k, :, :].rearrange("p a e -> p (a e)"),
                                     hT_hi[:, h, k, :], start=(k == 0), stop=False, skip_group_check=True)
                for k in range(KD):
                    last = nc.tensor.matmul(y[h][0][0:EXPERTS2, :], router_hl[:, k, 0, :], hT_lo[:, h, k, :],
                                            start=False, stop=(k == KD - 1), skip_group_check=True)
                last.then_inc(scored, 1)

            def transpose_scores(h):
                pe.wait_ge(score_rows_done, h + 1)
                for i in range(HALF_TILES):
                    last = nc.tensor.transpose(y[h][1][:, i * 2 * EXPERTS2:(i + 1) * 2 * EXPERTS2],
                                               score_rows[:, i * P:(i + 1) * P], ident[0:2 * EXPERTS2, 0:2 * EXPERTS2])
                last.then_inc(scores_T, 1)

            def up(q):
                b, h, c = STEPS[q]
                wait_lo(pe, b, c)
                if q >= len(z) and b == 0:
                    pe.wait_ge(act_done, q - len(z) + 1)
                elif b == 1 and q < FIRST[1, 0] + 2:
                    pe.wait_ge(act_done, 2 * q - FIRST[1, 0] - 2)
                elif b == 1:
                    pe.wait_ge(silu_done, q - 1)
                    pe.wait_ge(gated_done, q - 1)
                for m, bank in enumerate(z_banks(q)):
                    for k in range(KD):
                        if c == 0 and m == 0:
                            pe.wait_ge(hT_hi_done, KD * ln_no(b, h) + k + 1)
                        cols = slice((m * KD + k) * P, (m * KD + k + 1) * P)
                        nc.tensor.matmul(bank[:], w_hi[b][:, c, cols], hT_hi[:, h, k, :], start=(k == 0), stop=False)
                        nc.tensor.matmul(bank[:], w_lo[b][:, c, cols], hT_hi[:, h, k, :], start=False, stop=False)
                        if c == 0 and m == 0:
                            pe.wait_ge(hT_lo_done, KD * ln_no(b, h) + k + 1)
                        last = nc.tensor.matmul(bank[:], w_hi[b][:, c, cols], hT_lo[:, h, k, :], start=False,
                                                stop=(k == KD - 1))
                last.then_inc(up_done, 1)

            def down(q):
                b, h, c = STEPS[q]
                pe.wait_ge(act_lo_done, q + 1)
                wd = slice(UP_COLS[b], PIECE[b])
                for i in range(HALF_TILES):
                    rows = slice(i * P, (i + 1) * P)
                    o = y[h][i // 2][:, (i % 2) * D:(i % 2 + 1) * D]
                    first = c == 0 and i % 2 == 0
                    for j, (a, w) in enumerate(((act_lo, w_hi), (act_hi, w_lo), (act_hi, w_hi))):
                        last = nc.tensor.matmul(o, a[:, q % BUFFERS, rows], w[b][:, c, wd], start=(first and j == 0),
                                                stop=(c == CHUNKS[b] - 1 and j == 2), skip_group_check=True)
                    if q == NSTEPS - 1 and i == 1:
                        last.then_inc(last_first_bank, 1)
                last.then_inc(down_done, 1)

            def warm():
                for _ in range(WARM):
                    nc.tensor.matmul(z[3][:], warm_sb[:, 0:P], warm_sb[:], start=True, stop=True)

            def stages(q, slot):
                for way in due("transpose_gates", q, slot):
                    transpose_gates(*way, gate_bank(*way))
                for bb, hh in due("transpose_tokens", q, slot):
                    if bb == 0:
                        pe.wait_ge(gate_done, 2)
                    else:
                        pe.wait_ge(x2_done, 2 * hh + 2)
                    transpose_tokens(bb, hh)
                for _, hh in due("scores", q, slot):
                    route_scores(hh)
                for _, hh in due("transpose_scores", q, slot):
                    transpose_scores(hh)

            pe.wait_ge(warm_in, 1)
            warm()
            pe.wait_ge(consts_in, 16)
            transpose_gates(0, 0, gate_bank(0, 0))
            transpose_tokens(0, 0)
            for q in range(NSTEPS + LAG):
                if q < NSTEPS:
                    up(q)
                stages(q, 0)
                if q >= LAG:
                    b, h, c = STEPS[q - LAG]
                    if c == 0:
                        if b == 0:
                            pe.wait_ge(hT_lo_done, KD * ln_no(0, h) + KD)
                        else:
                            pe.wait_ge(gate_done, ln_no(1, h) + 1)
                    down(q - LAG)
                stages(q, 1)


def kernel(x, itok_BxS_13_99985, ctx_2048, L0_ffn_Wg, L0_ffn_W1, L0_ffn_W2, L0_ffn_W3):
    import numpy as np
    import concourse.bacc as bacc
    from concourse.bass_utils import run_bass_kernel_spmd

    c1, c2 = CHUNKS
    ctx = np.asarray(ctx_2048)
    up1 = ctx.reshape(EXPERTS1, c1, ROWS[0], KD, P).transpose(4, 1, 3, 0, 2).reshape(P, c1, KD * P)
    down1 = ctx.reshape(EXPERTS1, D, c1, ROWS[0]).transpose(0, 3, 2, 1).reshape(P, c1, D)
    ups2 = [np.asarray(w).reshape(EXPERTS2, c2, ROWS[1], KD, P).transpose(4, 1, 3, 0, 2).reshape(P, c2, KD * P)
            for w in (L0_ffn_W1, L0_ffn_W2)]
    down2 = np.asarray(L0_ffn_W3).reshape(EXPERTS2, D, c2, ROWS[1]).transpose(0, 3, 2, 1).reshape(P, c2, D)
    consts = np.zeros((P, CONSTS), np.float32)
    consts[:, C_IDENT:C_IDENT + P] = np.eye(P)
    consts[:, C_IOTA:] = np.arange(EXPERTS2)
    arrays = {
        "x_dram": np.ascontiguousarray(np.asarray(x).reshape(TOKENS, D)),
        "token_ids_dram": np.ascontiguousarray(np.asarray(itok_BxS_13_99985).reshape(P, TILES)),
        "weights1_dram": np.ascontiguousarray(np.concatenate([up1, down1], axis=2)),
        "weights2_dram": np.ascontiguousarray(np.concatenate([*ups2, down2], axis=2)),
        "router_dram": np.ascontiguousarray(np.asarray(L0_ffn_Wg).reshape(EXPERTS2, KD, P).transpose(2, 1, 0)),
        "consts_dram": consts,
    }
    nc = bacc.Bacc("TRN2", target_bir_lowering=False, num_devices=1)
    ins = [nc.dram_tensor(n, a.shape, mybir.dt.from_np(a.dtype), kind="ExternalInput").ap() for n, a in arrays.items()]
    out = nc.dram_tensor("out_dram", (TOKENS, D), F32, kind="ExternalOutput").ap()
    ffn_moe(nc, *ins, out)
    r = run_bass_kernel_spmd(nc, [arrays], core_ids=[0])
    return r.results[0]["out_dram"].reshape(np.asarray(x).shape)
```
